# Optimizing a Trainium2 kernel written in Bass

```python
import numpy as np
import jax
import jax.numpy as jnp

def _softmax(x, axis=-1):
    return jax.nn.softmax(x, axis=axis)
def _gelu(x):
    return jax.nn.gelu(x, approximate=True)
def _silu(x):
    return jax.nn.silu(x)
def _sigmoid(x):
    return jax.nn.sigmoid(x)
def _layernorm(x, axis=-1, eps=1e-5):
    m = jnp.mean(x, axis=axis, keepdims=True)
    v = jnp.var(x, axis=axis, keepdims=True)
    return (x - m) / jnp.sqrt(v + eps)
def _scatter_add(tgt, idx, src, axis=0):
    return tgt.at[idx].add(src)
def _segment_sum(src, seg, n):
    return jax.ops.segment_sum(src, seg, n)

kernel_name = 'mk_conv_preact_d1_conv_nchw64_01a86f'

def setup_inputs(seed: int = 0):
    np.random.seed(seed)
    _w = jnp.asarray
    def _rec_inputs():
        import jax
        import jax.numpy as jnp
        _gk = jax.random.key(seed)
        x = -0.000125 + 0.9999 * jax.random.normal(jax.random.fold_in(_gk, 1), (2048, 64, 16, 16), jnp.float32)
        return x
    x = _rec_inputs()
    def _L0_conv_setup():
        import jax
        import jax.numpy as jnp
        import numpy as np
        DST_R = np.array([1, 1, 2, 3, 4, 4, 6, 7, 8, 10, 11, 12, 14, 14, 15, 16, 17, 17, 16, 15, 14, 14, 12, 10, 8, 6, 4, 4, 3, 2])
        DST_C = np.array([3, 5, 7, 9, 10, 11, 13, 13, 14, 15, 15, 16, 15, 16, 15, 14, 13, 11, 9, 7, 6, 5, 3, 2, 1, 0, 0, 1, 1, 2])
        SRC_R = np.array([13, 13, 14, 15, 16, 16, 6, 7, 8, 10, 11, 12, 2, 2, 3, 4, 5, 5, 4, 3, 2, 2, 12, 10, 8, 6, 16, 16, 15, 14])
        SRC_C = np.array([15, 5, 7, 9, 10, 11, 1, 1, 2, 3, 3, 4, 3, 4, 3, 2, 1, 11, 9, 7, 6, 5, 15, 14, 13, 12, 12, 13, 13, 14])
        _UP = np.zeros((4, 4), np.float32)
        _UP[[0, 0, 1, 2, 2], [0, 1, 1, 1, 2]] = 1
        _LEFT = np.zeros((4, 4), np.float32)
        _LEFT[[1, 2, 2, 2, 3], [1, 0, 1, 2, 1]] = 1
        _RIGHT = np.zeros((4, 4), np.float32)
        _RIGHT[[1, 2, 2, 2, 3], [1, 1, 2, 3, 3]] = 1

        def _out_mask():
            m = np.ones((16, 16), np.float32)
            for i in range(9):
                m[i, 7 + i:16] = 0
            for i in range(7):
                m[9 + i, 0:i + 1] = 0
            m[0, 4:7] = 0
            m[1, 6:8] = 0
            m[2, 8] = 0
            m[3, 9] = 0
            m[6, 12] = 0
            m[7, 13] = 0
            m[8, 14] = 0
            m[9, 14] = 0
            m[10, 14] = 0
            m[11, 15] = 0
            m[13:, 14:] = 0
            m[15, 13] = 0
            m[15, 7:9] = 0
            m[13, 5] = 0
            m[14, 6] = 0
            m[8, 0] = 0
            m[9, 1] = 0
            m[7, 0] = 0
            m[3, 0] = 0
            m[0:3, 0:2] = 0
            m[0, 2] = 0
            return m
        OUT_MASK = _out_mask()

        def _conv(x, w, b):
            y = jax.lax.conv_general_dilated(x, w, window_strides=(2, 2), padding='VALID', dimension_numbers=('NCHW', 'OIHW', 'NCHW'))
            return y + b[None, :, None, None]
        key = jax.random.key(seed)
        ks = jax.random.split(key, 7)
        B, C, O = (2048, 64, 64)
        x = jax.random.normal(ks[0], (B, C, 16, 16), dtype=jnp.float32)
        w_up = jax.random.normal(ks[1], (O, C, 4, 4), dtype=jnp.float32) * 0.05
        b_up = jax.random.normal(ks[2], (O,), dtype=jnp.float32) * 0.05
        w_left = jax.random.normal(ks[3], (O, C, 4, 4), dtype=jnp.float32) * 0.05
        b_left = jax.random.normal(ks[4], (O,), dtype=jnp.float32) * 0.05
        w_right = jax.random.normal(ks[5], (O, C, 4, 4), dtype=jnp.float32) * 0.05
        b_right = jax.random.normal(ks[6], (O,), dtype=jnp.float32) * 0.05
        return {'x': x, 'w_up': w_up, 'b_up': b_up, 'w_left': w_left, 'b_left': b_left, 'w_right': w_right, 'b_right': b_right}
    _L0_conv_all = _L0_conv_setup()
    _L0_conv_in = {k: v for k, v in _L0_conv_all.items() if k in ('w_up', 'b_up', 'w_left', 'b_left', 'w_right', 'b_right', )}
    del _L0_conv_all

    return {
        "x": x,
        "L0_conv_w_up": _L0_conv_in["w_up"],
        "L0_conv_b_up": _L0_conv_in["b_up"],
        "L0_conv_w_left": _L0_conv_in["w_left"],
        "L0_conv_b_left": _L0_conv_in["b_left"],
        "L0_conv_w_right": _L0_conv_in["w_right"],
        "L0_conv_b_right": _L0_conv_in["b_right"],
    }

def reference(x, L0_conv_w_up, L0_conv_b_up, L0_conv_w_left, L0_conv_b_left, L0_conv_w_right, L0_conv_b_right):
    import jax
    import jax.numpy as jnp
    def _L0_conv_ref(x, w_up, b_up, w_left, b_left, w_right, b_right):
        import jax
        import jax.numpy as jnp
        import numpy as np
        DST_R = np.array([1, 1, 2, 3, 4, 4, 6, 7, 8, 10, 11, 12, 14, 14, 15, 16, 17, 17, 16, 15, 14, 14, 12, 10, 8, 6, 4, 4, 3, 2])
        DST_C = np.array([3, 5, 7, 9, 10, 11, 13, 13, 14, 15, 15, 16, 15, 16, 15, 14, 13, 11, 9, 7, 6, 5, 3, 2, 1, 0, 0, 1, 1, 2])
        SRC_R = np.array([13, 13, 14, 15, 16, 16, 6, 7, 8, 10, 11, 12, 2, 2, 3, 4, 5, 5, 4, 3, 2, 2, 12, 10, 8, 6, 16, 16, 15, 14])
        SRC_C = np.array([15, 5, 7, 9, 10, 11, 1, 1, 2, 3, 3, 4, 3, 4, 3, 2, 1, 11, 9, 7, 6, 5, 15, 14, 13, 12, 12, 13, 13, 14])
        _UP = np.zeros((4, 4), np.float32)
        _UP[[0, 0, 1, 2, 2], [0, 1, 1, 1, 2]] = 1
        _LEFT = np.zeros((4, 4), np.float32)
        _LEFT[[1, 2, 2, 2, 3], [1, 0, 1, 2, 1]] = 1
        _RIGHT = np.zeros((4, 4), np.float32)
        _RIGHT[[1, 2, 2, 2, 3], [1, 1, 2, 3, 3]] = 1

        def _out_mask():
            m = np.ones((16, 16), np.float32)
            for i in range(9):
                m[i, 7 + i:16] = 0
            for i in range(7):
                m[9 + i, 0:i + 1] = 0
            m[0, 4:7] = 0
            m[1, 6:8] = 0
            m[2, 8] = 0
            m[3, 9] = 0
            m[6, 12] = 0
            m[7, 13] = 0
            m[8, 14] = 0
            m[9, 14] = 0
            m[10, 14] = 0
            m[11, 15] = 0
            m[13:, 14:] = 0
            m[15, 13] = 0
            m[15, 7:9] = 0
            m[13, 5] = 0
            m[14, 6] = 0
            m[8, 0] = 0
            m[9, 1] = 0
            m[7, 0] = 0
            m[3, 0] = 0
            m[0:3, 0:2] = 0
            m[0, 2] = 0
            return m
        OUT_MASK = _out_mask()

        def _conv(x, w, b):
            y = jax.lax.conv_general_dilated(x, w, window_strides=(2, 2), padding='VALID', dimension_numbers=('NCHW', 'OIHW', 'NCHW'))
            return y + b[None, :, None, None]
        xp = jnp.pad(x, ((0, 0), (0, 0), (1, 1), (1, 1)))
        xp = xp.at[:, :, DST_R, DST_C].set(xp[:, :, SRC_R, SRC_C])
        up = _conv(xp, w_up * jnp.asarray(_UP), b_up)
        left = _conv(xp, w_left * jnp.asarray(_LEFT), b_left)
        right = _conv(xp, w_right * jnp.asarray(_RIGHT), b_right)
        B, O = (up.shape[0], up.shape[1])
        out = jnp.zeros((B, O, 16, 16), x.dtype)
        out = out.at[:, :, 0::2, 0::2].set(up)
        out = out.at[:, :, 1::2, 0::2].set(left)
        out = out.at[:, :, 1::2, 1::2].set(right)
        return out * jnp.asarray(OUT_MASK)

    def _gn(v, G=32, eps=1e-5):
        B_, C_, H_, W_ = v.shape
        g = v.reshape(B_, G, C_ // G, H_, W_)
        m = jnp.mean(g, axis=(2, 3, 4), keepdims=True)
        s = jnp.var(g, axis=(2, 3, 4), keepdims=True)
        return ((g - m) / jnp.sqrt(s + eps)).reshape(v.shape)

    def _ln_c(v, eps=1e-6):
        m = jnp.mean(v, axis=1, keepdims=True)
        s = jnp.var(v, axis=1, keepdims=True)
        return (v - m) / jnp.sqrt(s + eps)

    def _ln_t(v, eps=1e-5):
        m = jnp.mean(v, axis=-1, keepdims=True)
        s = jnp.var(v, axis=-1, keepdims=True)
        return (v - m) / jnp.sqrt(s + eps)

    def _to_tokens(v):
        B_, C_, H_, W_ = v.shape
        return v.reshape(B_, C_, H_ * W_).transpose(0, 2, 1)
    def _from_tokens(t, like):
        B_, C_, H_, W_ = like.shape
        return t.transpose(0, 2, 1).reshape(B_, C_, H_, W_)

    x = x + _L0_conv_ref(_gn(x), L0_conv_w_up, L0_conv_b_up, L0_conv_w_left, L0_conv_b_left, L0_conv_w_right, L0_conv_b_right)
    return x


_drawn_inputs = setup_inputs


def setup_inputs(seed=0):
    import zlib

    import numpy as np

    out = dict(_drawn_inputs(seed))
    spreads = {}
    factors = {'L0_conv_b_up': 3.672, 'L0_conv_b_left': 3.646, 'L0_conv_b_right': 3.064}
    for name, (base, spread) in spreads.items():
        noise = np.random.default_rng([zlib.crc32(name.encode()), seed]).standard_normal(out[name].shape)
        drawn = base * np.exp(spread * noise) if base else spread * noise
        out[name] = jnp.asarray(drawn.astype(out[name].dtype))
    for name, factor in factors.items():
        out[name] = (out[name] * factor).astype(out[name].dtype)
    return out
```

```python
from contextlib import ExitStack

import concourse.bass as bass
import numpy as np
from concourse import mybir

F32 = mybir.dt.float32
F16 = mybir.dt.float16
I32 = mybir.dt.int32
ALU = mybir.AluOpType
ACT = mybir.ActivationFunctionType
AX = mybir.AxisListType

P = 128
B, C, HW = 2048, 64, 16
PIX = HW * HW
G = 16
NCHUNK = B // (2 * G)
SLOTS = 8
ROUNDS = NCHUNK // SLOTS
LAG = 2
GD = 8
EPS = 1e-5
GROUP = 2 * PIX

X_SCALE = 2048.0
W_SCALE = 512.0

TP = 18
T_PAIR = 17 * TP
H_PAIR = 8 * 27 + 9


def t_at(r, c):
    return TP * (r - 1) + c


def h_at(r, c):
    return 27 * (r // 2) - 18 + c if r % 2 == 0 else 27 * (r // 2) + (c - 1) // 2


UP, LEFT, RIGHT = range(3)
TAPS = [
    [(0, 0), (0, 1), (1, 1), (2, 1), (2, 2)],
    [(1, 1), (2, 0), (2, 1), (2, 2), (3, 1)],
    [(1, 1), (2, 1), (2, 2), (2, 3), (3, 3)],
]
OUT_AT = [(0, 0), (1, 0), (1, 1)]
NT = 5
NTAP = 3 * NT
NPART = 2 * NTAP

BANKS = [
    [(UP, 2, 0, 3, 2, 1, 6, (6,)), (UP, 3, 0, 2, 2, 1, 6, (6,))],
    [(LEFT, 2, 0, 2, 2, 1, 6, (6,)), (LEFT, 3, 1, 2, 2, 1, 6, (6,)), (LEFT, 1, 1, 2, 5, 2, 4, (4,))],
    [(RIGHT, 2, 0, 2, 2, 1, 7, (6, 7)), (RIGHT, 3, 0, 2, 2, 1, 6, (6,)), (RIGHT, 0, 1, 2, 7, 3, 2, (2,))],
    [(UP, 1, 1, 2, 6, 3, 3, (3,)), (LEFT, 0, 1, 2, 7, 4, 2, (2,)), (RIGHT, 1, 0, 2, 5, 3, 4, (4,))],
]
NB = len(BANKS)
BANK_COLS = [sum(r[3] * r[6] for r in rects) * G for rects in BANKS]
BANK_AT = [sum(BANK_COLS[:j]) for j in range(NB)]

PIECES = [
    (4, -1, 6, 2, 1, 14), (3, -1, 4, 4, 2, 8), (5, 1, 3, 4, 2, 7),
    (2, 2, 2, 14, 7, 6), (1, 3, 2, 16, 8, 2), (10, 16, 1, 2, 1, 1),
]

WRAPS = [
    (t_at(1, 3), t_at(13, 15), [(13 * TP + 13, -11 * TP - 11, 2), (TP - 1, TP - 1, 4)]),
    (t_at(1, 5), t_at(13, 5), [(13 * TP, -11 * TP, 2), (TP + 2, TP + 2, 4)]),
    (t_at(6, 0), t_at(6, 12), [(13, -11, 2), (2 * TP + 1, 2 * TP + 1, 4)]),
    (t_at(4, 1), t_at(16, 13), [(10 * TP + 5, -14 * TP - 7, 2), (9, -3, 2)]),
    (t_at(7, 13), t_at(7, 1), [(4 * TP + 2, 4 * TP + 2, 2)]),
]

PREP_BANKS = 8
STAT_OPS = 11


def starts(k):
    return isinstance(k, int) and k == 0


def view(tensor, at, dims, first=0, parts=P):
    full = tensor[:, ]
    row = full.ap[0][0]
    return bass.AP(full.tensor, full.offset + first * row + at, [[row, parts]] + [list(d) for d in dims])


def hex_conv(nc, x, w_up, b_up, w_left, b_left, w_right, b_right, out):
    ctx = ExitStack()
    with ctx:
        def sb(name, shape, dt):
            return ctx.enter_context(nc.sbuf_tensor(name, shape, dt))

        def sem(name):
            return ctx.enter_context(nc.semaphore(name))

        x_dram = x.rearrange("(n g h) c r q -> n (h c) g (r q)", g=G, h=2)
        out_dram = out.rearrange("(n g h) c r q -> n (h c) g (r q)", g=G, h=2)

        xs = sb("xs", [P, SLOTS, G * PIX], F32)
        tn = sb("tn", [P, G * T_PAIR], F32)
        hi = [sb(f"hi{b}", [P, G * H_PAIR], F16) for b in range(2)]
        lo = [sb(f"lo{b}", [P, G * H_PAIR], F16) for b in range(2)]
        wts = sb("wts", [P, NPART, P], F16)
        res = sb("res", [P, sum(BANK_COLS)], F32)
        ident = sb("ident", [P, P], F16)
        bias = sb("bias", [P, 3], F32)
        stats = sb("stats", [P, G, 12], F32)
        msum = sb("msum", [P, G], F32)
        dev = sb("dev", [P, G, 4], F32)
        vsum = sb("vsum", [P, G], F32)
        var = sb("var", [P, G], F32)
        std = sb("std", [P, G], F32)
        small = sb("small", [P, 4, G], F32)
        rstd = sb("rstd", [P, G], F32)
        nmr = sb("nmr", [P, G], F32)
        wmax = sb("wmax", [P, 6], F32)
        psum = [ctx.enter_context(nc.psum_tensor(f"bank{j}", [P, 512], F32)) for j in range(2 * NB)]

        raw = xs[:, SLOTS - 1, 0:3 * C * 16]
        raw_v = raw.rearrange("p (t c k) -> p t c k", t=3, k=16)
        used = xs[:, SLOTS - 2, 0:NTAP * C]
        used_v = used.rearrange("p (n c) -> p n c", n=NTAP)
        blocks = xs[:, SLOTS - 2, NTAP * C:3 * NTAP * C].bitcast(F16)
        blocks_v = blocks.rearrange("p (n c) -> p n c", n=NPART)

        loaded = [sem(f"loaded{s}") for s in range(SLOTS)]
        stored = [sem(f"stored{s}") for s in range(SLOTS)]
        w_loaded = sem("w_loaded")
        cleared = sem("cleared")
        taps_used = sem("taps_used")
        w_step = sem("w_step")
        w_scaled = sem("w_scaled")
        w_high = sem("w_high")
        w_low = sem("w_low")
        bn_done = sem("bn_done")
        stat_step = sem("stat_step")
        var_ready = sem("var_ready")
        std_ready = sem("std_ready")
        norm_ready = sem("norm_ready")
        t_dve = sem("t_dve")
        t_act = sem("t_act")
        t_ready = sem("t_ready")
        hi_ready = sem("hi_ready")
        lo_ready = sem("lo_ready")
        bank_full = sem("bank_full")
        bank_empty = sem("bank_empty")
        bank_added = sem("bank_added")

        def t_image(g):
            return view(tn, g * T_PAIR + t_at(2, 1), [(TP, 15), (1, HW)])

        def x_image(s, g):
            return xs[:, s, g * PIX + HW:(g + 1) * PIX].rearrange("p (r q) -> p r q", q=HW)

        def t_piece(piece):
            r, c, rows, dr, dc, w = piece
            return view(tn, t_at(r, c), [(T_PAIR, G), (dr * TP + dc, rows), (1 + r % 2, w)])

        def h_piece(part, piece):
            r, c, rows, dr, dc, w = piece
            step = 27 * (dr // 2) + (dc if r % 2 == 0 else dc // 2)
            return view(part, h_at(r, c), [(H_PAIR, G), (step, rows), (1, w)])

        block = ctx.enter_context(nc.Block())

        @block.sync
        def _(sp):
            def load(i, s):
                sp.dma_start(xs[:, s, :].rearrange("p (g q) -> p g q", g=G),
                             x_dram[SLOTS * i + s]).then_inc(loaded[s], 16)

            def store(i, s):
                sp.wait_ge(bank_added, NB * (SLOTS * i + s + 1))
                sp.dma_start(out_dram[SLOTS * i + s],
                             xs[:, s, :].rearrange("p (g q) -> p g q", g=G)).then_inc(stored[s], 16)

            load(0, 0)
            for t, w in enumerate((w_up, w_left, w_right)):
                for h in range(2):
                    sp.dma_start(raw[C * h:C * h + C, t * C * 16:(t + 1) * C * 16],
                                 w.rearrange("o c a b -> o (c a b)")).then_inc(w_loaded, 16)
            for t, b in enumerate((b_up, b_left, b_right)):
                for h in range(2):
                    sp.dma_start(bias[C * h:C * h + C, t:t + 1],
                                 b.rearrange("(o a) -> o a", a=1)).then_inc(w_loaded, 16)
            for s in range(1, SLOTS - 2):
                load(0, s)
            sp.wait_ge(bank_empty, PREP_BANKS)
            load(0, SLOTS - 2)

            def step(i, s, more=True):
                store(i, s)
                if s:
                    if more:
                        sp.wait_ge(stored[s - 1], 16 * (i + 1))
                        load(i + 1, s - 1)
                else:
                    if not starts(i):
                        sp.wait_ge(stored[SLOTS - 1], 16 * i)
                    load(i, SLOTS - 1)

            for s in range(SLOTS):
                step(0, s)
            with sp.Fori(1, ROUNDS - 1) as i:
                for s in range(SLOTS):
                    step(i, s)
            for s in range(SLOTS):
                step(ROUNDS - 1, s, more=False)
            for s in range(SLOTS):
                sp.wait_ge(stored[s], 16 * ROUNDS)

        @block.vector
        def _(dve):
            def bn(i, s, g0, g1):
                if g0 == 0:
                    dve.wait_ge(loaded[s], 16 * (i + 1))
                for g in range(g0, g1):
                    last = nc.vector.bn_stats(stats[:, g, 0:6], xs[:, s, g * PIX:(g + 1) * PIX])
                if g1 == G:
                    last.then_inc(bn_done, 1)

            def moments(k):
                done = STAT_OPS * k
                means = stats[:, :, 1:11:3]
                m2s = stats[:, :, 2:12:3]
                nc.vector.stream_shuffle(stats[:, :, 6:12], stats[:, :, 0:6],
                                         [p ^ 1 for p in range(32)]).then_inc(stat_step, 1)
                dve.wait_ge(stat_step, done + 1)
                nc.vector.reduce_sum(msum[:], means, axis=AX.X).then_inc(stat_step, 1)
                dve.wait_ge(stat_step, done + 2)
                nc.vector.scalar_tensor_tensor(dev[:], msum[:].unsqueeze(2).to_broadcast([P, G, 4]), -0.25, means,
                                               op0=ALU.mult, op1=ALU.add).then_inc(stat_step, 1)
                dve.wait_ge(stat_step, done + 3)
                nc.vector.tensor_tensor(dev[:], dev[:], dev[:], ALU.mult).then_inc(stat_step, 1)
                dve.wait_ge(stat_step, done + 4)
                nc.vector.scalar_tensor_tensor(dev[:], dev[:], float(PIX // 2), m2s,
                                               op0=ALU.mult, op1=ALU.add).then_inc(stat_step, 1)
                dve.wait_ge(stat_step, done + 5)
                nc.vector.reduce_sum(vsum[:], dev[:], axis=AX.X).then_inc(stat_step, 1)
                dve.wait_ge(stat_step, done + 6)
                nc.vector.tensor_scalar(var[:], vsum[:], 1.0 / GROUP, EPS,
                                        ALU.mult, ALU.add).then_inc(var_ready, 1)

            def norms(k):
                done = STAT_OPS * k + 6
                dve.wait_ge(std_ready, k + 1)
                nc.vector.reciprocal(small[:, 0], std[:]).then_inc(stat_step, 1)
                dve.wait_ge(stat_step, done + 1)
                nc.vector.tensor_tensor(small[:, 1], small[:, 0], small[:, 0], ALU.mult).then_inc(stat_step, 1)
                dve.wait_ge(stat_step, done + 2)
                nc.vector.tensor_tensor(small[:, 2], small[:, 1], var[:], ALU.mult).then_inc(stat_step, 1)
                dve.wait_ge(stat_step, done + 3)
                nc.vector.tensor_scalar(small[:, 3], small[:, 2], -0.5 * X_SCALE, 1.5 * X_SCALE,
                                        ALU.mult, ALU.add).then_inc(stat_step, 1)
                dve.wait_ge(stat_step, done + 4)
                nc.vector.tensor_tensor(rstd[:], small[:, 3], small[:, 0], ALU.mult).then_inc(stat_step, 1)
                dve.wait_ge(stat_step, done + 5)
                nc.vector.scalar_tensor_tensor(nmr[:], msum[:], -0.25, rstd[:],
                                               op0=ALU.mult, op1=ALU.mult).then_inc(norm_ready, 1)

            def normalise(k, s):
                dve.wait_ge(norm_ready, k + 1)
                if starts(k):
                    dve.wait_ge(cleared, 2)
                else:
                    dve.wait_ge(lo_ready, k)
                for g in range(GD):
                    last = nc.vector.tensor_scalar(t_image(g), x_image(s, g), rstd[:, g:g + 1], nmr[:, g:g + 1],
                                                   ALU.mult, ALU.add)
                last.then_inc(t_dve, 1)

            def wrap(k, more):
                dve.wait_ge(t_dve, k + 1)
                dve.wait_ge(t_act, k + 1)
                for n, (dst, src, dims) in enumerate(WRAPS):
                    if more and n == len(WRAPS) - 1:
                        dve.wait_ge(bn_done, k + 2)
                    last = nc.vector.tensor_copy(view(tn, dst, [(T_PAIR, G)] + [(d, n) for d, _, n in dims]),
                                                 view(tn, src, [(T_PAIR, G)] + [(d, n) for _, d, n in dims]))
                last.then_inc(t_ready, 1)

            def step(i, s, more=True):
                k = SLOTS * i + s
                ahead = (i, s + 1) if s < SLOTS - 1 else (i + 1, 0)
                moments(k)
                if more:
                    bn(*ahead, 0, G // 2)
                norms(k)
                normalise(k, s)
                if more:
                    bn(*ahead, G // 2, G)
                wrap(k, more)

            bn(0, 0, 0, G)
            dve.wait_ge(bn_done, 1)

            dve.wait_ge(taps_used, 1)
            nc.vector.reduce_max(wmax[:, 0:1], used, axis=AX.X, apply_absolute_value=True).then_inc(w_step, 1)
            dve.wait_ge(w_step, 1)
            nc.vector.tensor_scalar(wmax[:, 1:2], wmax[:, 0:1], 1e-30, None, ALU.max).then_inc(w_step, 1)
            dve.wait_ge(w_step, 2)
            nc.vector.tensor_scalar(wmax[:, 2:3].bitcast(I32), wmax[:, 1:2].bitcast(I32), 0x7F800000, None,
                                    ALU.bitwise_and).then_inc(w_step, 1)
            dve.wait_ge(w_step, 3)
            nc.vector.reciprocal(wmax[:, 3:4], wmax[:, 2:3]).then_inc(w_step, 1)
            nc.vector.tensor_scalar(wmax[:, 5:6], wmax[:, 2:3], 1.0 / (W_SCALE * X_SCALE), None,
                                    ALU.mult).then_inc(w_step, 1)
            dve.wait_ge(w_step, 4)
            nc.vector.tensor_scalar(wmax[:, 4:5], wmax[:, 3:4], W_SCALE, None, ALU.mult).then_inc(w_step, 1)
            dve.wait_ge(w_step, 6)
            nc.vector.tensor_scalar(used, used, wmax[:, 4:5], None, ALU.mult).then_inc(w_scaled, 1)

            for s in range(SLOTS):
                step(0, s)
            with dve.Fori(1, ROUNDS - 1) as i:
                for s in range(SLOTS):
                    step(i, s)
            for s in range(SLOTS):
                step(ROUNDS - 1, s, more=s < SLOTS - 1)

        @block.scalar
        def _(act):
            def root(k):
                act.wait_ge(var_ready, k + 1)
                nc.scalar.activation(std[:], var[:], ACT.Sqrt).then_inc(std_ready, 1)

            def normalise(k, s, g0, g1):
                if g0 == GD:
                    act.wait_ge(norm_ready, k + 1)
                    if starts(k):
                        act.wait_ge(cleared, 2)
                    else:
                        act.wait_ge(lo_ready, k)
                for g in range(g0, g1):
                    last = nc.scalar.activation(t_image(g), x_image(s, g), ACT.Identity,
                                                bias=nmr[:, g:g + 1], scale=rstd[:, g:g + 1])
                if g1 == G:
                    last.then_inc(t_act, 1)

            def high(k, b):
                act.wait_ge(t_ready, k + 1)
                act.wait_ge(bank_full, PREP_BANKS + NB * (k - 1))
                for piece in PIECES:
                    last = nc.scalar.copy(h_piece(hi[b], piece), t_piece(piece))
                last.then_inc(hi_ready, 1)

            def evacuate(k, b, j):
                act.wait_ge(bank_full, PREP_BANKS + NB * k + j + 1)
                if not starts(k):
                    act.wait_ge(bank_added, NB * (k - 1) + j + 1)
                at = 0
                for n, rect in enumerate(BANKS[j]):
                    cols = rect[3] * rect[6] * G
                    if n and rect[0] == BANKS[j][n - 1][0]:
                        continue
                    cols = sum(q[3] * q[6] * G for q in BANKS[j][n:] if q[0] == rect[0])
                    last = nc.scalar.activation(res[:, BANK_AT[j] + at:BANK_AT[j] + at + cols],
                                                psum[NB * b + j][:, at:at + cols], ACT.Identity,
                                                bias=bias[:, rect[0]:rect[0] + 1], scale=wmax[:, 5:6])
                    at += cols
                last.then_inc(bank_empty, 1)

            def step(i, s, old=True):
                k = SLOTS * i + s
                root(k)
                if old:
                    evacuate(k - LAG, s % 2, 0)
                    evacuate(k - LAG, s % 2, 1)
                normalise(k, s, GD, GD + 4)
                if old:
                    evacuate(k - LAG, s % 2, 2)
                    evacuate(k - LAG, s % 2, 3)
                normalise(k, s, GD + 4, G)
                high(k, s % 2)

            act.wait_ge(w_loaded, 16 * 12)
            for t in range(3):
                for n, (a, b) in enumerate(TAPS[t]):
                    last = nc.scalar.copy(used_v[:, t * NT + n], raw_v[:, t, :, 4 * a + b])
            last.then_inc(taps_used, 1)
            act.wait_ge(w_scaled, 1)
            act.wait_ge(cleared, 1)
            for h in range(2):
                rows = slice(C * h, C * h + C)
                last = nc.scalar.copy(blocks_v[rows, 0:NTAP, rows], used_v[rows])
            last.then_inc(w_high, 1)
            for j in range(PREP_BANKS):
                n = min(4, NPART - 4 * j)
                act.wait_ge(bank_full, j + 1)
                nc.scalar.copy(wts[:, 4 * j:4 * j + n, :].rearrange("p n o -> p (n o)"),
                               psum[j][:, 0:n * P]).then_inc(bank_empty, 1)

            for s in range(SLOTS):
                step(0, s, old=s >= LAG)
            with act.Fori(1, ROUNDS) as i:
                for s in range(SLOTS):
                    step(i, s)
            for k in range(NCHUNK - LAG, NCHUNK):
                for j in range(NB):
                    evacuate(k, k % 2, j)

        @block.gpsimd
        def _(pool):
            nc.gpsimd.memset(blocks.bitcast(F32), 0.0)
            nc.gpsimd.memset(ident[:], 0.0).then_inc(cleared, 1)
            pool.wait_ge(cleared, 1)
            nc.gpsimd.affine_select(out=ident[:], in_=ident[:], compare_op=ALU.not_equal, fill=1.0,
                                    base=0, pattern=[[-1, P]], channel_multiplier=1)
            for part in (*hi, *lo):
                nc.gpsimd.memset(part[:].bitcast(F32), 0.0)
            nc.gpsimd.memset(tn[:], 0.0).then_inc(cleared, 1)

            pool.wait_ge(cleared, 2)
            pool.wait_ge(w_high, 1)
            for h in range(2):
                rows = slice(C * h, C * h + C)
                nc.gpsimd.tensor_tensor(blocks_v[rows, NTAP:NPART, rows], used_v[rows],
                                        blocks_v[rows, 0:NTAP, rows], ALU.subtract).then_inc(w_low, 1)
                pool.wait_ge(w_low, h + 1)

            def low(k, b):
                pool.wait_ge(hi_ready, k + 1)
                for piece in PIECES:
                    last = nc.gpsimd.tensor_tensor(h_piece(lo[b], piece), t_piece(piece),
                                                   h_piece(hi[b], piece), ALU.subtract)
                last.then_inc(lo_ready, 1)

            def add(k, s, j):
                pool.wait_ge(bank_empty, PREP_BANKS + NB * k + j + 1)
                at = BANK_AT[j]
                for t, r0, c0, rows, dr, dc, w, kept in BANKS[j]:
                    x0 = s * G * PIX + HW * (2 * r0 + OUT_AT[t][0]) + 2 * c0 + OUT_AT[t][1]
                    xstep = 2 * HW * dr + 2 * dc
                    pieces = [(0, rows, 0, kept[0])]
                    if kept[-1] > kept[0]:
                        pieces.append((rows - 1, 1, kept[0], kept[-1] - kept[0]))
                    for row, nrow, col, width in pieces:
                        onto = view(xs, x0 + row * xstep + 2 * col, [(PIX, G), (xstep, nrow), (2, width)])
                        last = nc.gpsimd.tensor_tensor(
                            onto, view(res, at + row * w + col, [(rows * w, G), (w, nrow), (1, width)]),
                            onto, ALU.add)
                    at += rows * w * G
                last.then_inc(bank_added, 1)

            def step(i, s, old=True):
                k = SLOTS * i + s
                if old:
                    for j in range(NB):
                        add(k - LAG, (s - LAG) % SLOTS, j)
                low(k, s % 2)

            for s in range(SLOTS):
                step(0, s, old=s >= LAG)
            with pool.Fori(1, ROUNDS) as i:
                for s in range(SLOTS):
                    step(i, s)
            for k in range(NCHUNK - LAG, NCHUNK):
                for j in range(NB):
                    add(k, k % SLOTS, j)

        @block.tensor
        def _(pe):
            pe.wait_ge(w_low, 2)
            pe.wait_ge(cleared, 2)
            for j in range(PREP_BANKS):
                for n in range(4 * j, min(4 * j + 4, NPART)):
                    last = nc.tensor.matmul(psum[j][:, (n - 4 * j) * P:(n - 4 * j + 1) * P], blocks_v[:, n, :],
                                            ident[:], start=True, stop=True)
                last.then_inc(bank_full, 1)
            pe.wait_ge(bank_empty, PREP_BANKS)

            def taps(part, rect, tap):
                t, r0, c0, rows, dr, dc, w, _ = rect
                r, c = 2 * r0 + tap[0], 2 * c0 + tap[1]
                odd = r % 2
                step = 27 * dr + (dc if odd else 2 * dc)
                return view(part, h_at(r, c), [(H_PAIR, G), (step, rows), (1 if odd else 2, w)])

            def convolve(k, b):
                pe.wait_ge(lo_ready, k + 1)
                for j, rects in enumerate(BANKS):
                    pe.wait_ge(bank_empty, NB * k + j + 1)
                    at = 0
                    for q, rect in enumerate(rects):
                        cols = rect[3] * rect[6] * G
                        for n, tap in enumerate(TAPS[rect[0]]):
                            for m, (wpart, xpart) in enumerate(((0, hi[b]), (0, lo[b]), (1, hi[b]))):
                                last = nc.tensor.matmul(
                                    psum[NB * b + j][:, at:at + cols], wts[:, wpart * NTAP + NT * rect[0] + n, :],
                                    taps(xpart, rect, tap), start=(q == 0 and n == 0 and m == 0),
                                    stop=(n == NT - 1 and m == 2), skip_group_check=True)
                        at += cols
                    last.then_inc(bank_full, 1)

            with pe.Fori(0, NCHUNK // 2) as i:
                for b in range(2):
                    convolve(2 * i + b, b)


_INS = ["x", "L0_conv_w_up", "L0_conv_b_up", "L0_conv_w_left", "L0_conv_b_left", "L0_conv_w_right", "L0_conv_b_right"]


def kernel(**inputs):
    import concourse.bacc as _bacc
    from concourse.bass_utils import run_bass_kernel_spmd as _run

    nc = _bacc.Bacc("TRN2", target_bir_lowering=False, num_devices=1)
    arrays, args = {}, []
    for name in _INS:
        a = np.ascontiguousarray(inputs[name])
        arrays[f"in_{name}"] = a
        args.append(nc.dram_tensor(f"in_{name}", a.shape, mybir.dt.from_np(a.dtype), kind="ExternalInput").ap())
    shape = arrays["in_x"].shape
    out = nc.dram_tensor("out_0", shape, F32, kind="ExternalOutput").ap()
    hex_conv(nc, *args, out)
    r = _run(nc, [arrays], core_ids=[0])
    return r.results[0]["out_0"]
```

```python
from contextlib import ExitStack

import concourse.bass as bass
import numpy as np
from concourse import mybir

F32 = mybir.dt.float32
F16 = mybir.dt.float16
I32 = mybir.dt.int32
ALU = mybir.AluOpType
ACT = mybir.ActivationFunctionType
AX = mybir.AxisListType

P = 128
B, C, HW = 2048, 64, 16
PIX = HW * HW
G = 16
NCHUNK = B // (2 * G)
SLOTS = 8
ROUNDS = NCHUNK // SLOTS
LAG = 2
GD = 7
GD0 = 10
EPS = 1e-5
GROUP = 2 * PIX

X_SCALE = 2048.0
W_SCALE = 512.0

TP = 18
T_PAIR = 17 * TP
H_PAIR = 8 * 27 + 9


def t_at(r, c):
    return TP * (r - 1) + c


def h_at(r, c):
    return 27 * (r // 2) - 18 + c if r % 2 == 0 else 27 * (r // 2) + (c - 1) // 2


UP, LEFT, RIGHT = range(3)
TAPS = [
    [(0, 0), (0, 1), (1, 1), (2, 1), (2, 2)],
    [(1, 1), (2, 0), (2, 1), (2, 2), (3, 1)],
    [(1, 1), (2, 1), (2, 2), (2, 3), (3, 3)],
]
OUT_AT = [(0, 0), (1, 0), (1, 1)]
NT = 5
NTAP = 3 * NT
NPART = 2 * NTAP

BANKS = [
    [(UP, 2, 0, 3, 2, 1, 6, (6,)), (UP, 3, 0, 2, 2, 1, 6, (6,))],
    [(LEFT, 2, 0, 2, 2, 1, 6, (6,)), (LEFT, 3, 1, 2, 2, 1, 6, (6,)), (LEFT, 1, 1, 2, 5, 2, 4, (4,))],
    [(RIGHT, 2, 0, 2, 2, 1, 7, (6, 7)), (RIGHT, 3, 0, 2, 2, 1, 6, (6,)), (RIGHT, 0, 1, 2, 7, 3, 2, (2,))],
    [(UP, 1, 1, 2, 6, 3, 3, (3,)), (LEFT, 0, 1, 2, 7, 4, 2, (2,)), (RIGHT, 1, 0, 2, 5, 3, 4, (4,))],
]
NB = len(BANKS)
BANK_COLS = [sum(r[3] * r[6] for r in rects) * G for rects in BANKS]
BANK_AT = [sum(BANK_COLS[:j]) for j in range(NB)]

PIECES = [
    (4, -1, 6, 2, 1, 14), (3, -1, 4, 4, 2, 8), (5, 1, 3, 4, 2, 7),
    (2, 2, 2, 14, 7, 6), (1, 3, 2, 16, 8, 2), (10, 16, 1, 2, 1, 1),
]

WRAPS = [
    (t_at(1, 3), t_at(13, 15), [(13 * TP + 13, -11 * TP - 11, 2), (TP - 1, TP - 1, 4)]),
    (t_at(1, 5), t_at(13, 5), [(13 * TP, -11 * TP, 2), (TP + 2, TP + 2, 4)]),
    (t_at(6, 0), t_at(6, 12), [(13, -11, 2), (2 * TP + 1, 2 * TP + 1, 4)]),
    (t_at(4, 1), t_at(16, 13), [(10 * TP + 5, -14 * TP - 7, 2), (9, -3, 2)]),
    (t_at(7, 13), t_at(7, 1), [(4 * TP + 2, 4 * TP + 2, 2)]),
]

PREP_BANKS = 8
STAT_OPS = 11


def starts(k):
    return isinstance(k, int) and k == 0


def view(tensor, at, dims, first=0, parts=P):
    full = tensor[:, ]
    row = full.ap[0][0]
    return bass.AP(full.tensor, full.offset + first * row + at, [[row, parts]] + [list(d) for d in dims])


def hex_conv(nc, x, w_up, b_up, w_left, b_left, w_right, b_right, out):
    ctx = ExitStack()
    with ctx:
        def sb(name, shape, dt):
            return ctx.enter_context(nc.sbuf_tensor(name, shape, dt))

        def sem(name):
            return ctx.enter_context(nc.semaphore(name))

        x_dram = x.rearrange("(n g h) c r q -> n (h c) g (r q)", g=G, h=2)
        out_dram = out.rearrange("(n g h) c r q -> n (h c) g (r q)", g=G, h=2)

        xs = sb("xs", [P, SLOTS, G * PIX], F32)
        tn = [sb(f"tn{b}", [P, G * T_PAIR], F32) for b in range(2)]
        hi = [sb(f"hi{b}", [P, G * H_PAIR], F16) for b in range(2)]
        lo = [sb(f"lo{b}", [P, G * H_PAIR], F16) for b in range(2)]
        wts = sb("wts", [P, NPART, P], F16)
        res = sb("res", [P, sum(BANK_COLS)], F32)
        ident = sb("ident", [P, P], F16)
        bias = sb("bias", [P, 3], F32)
        stats = sb("stats", [P, 2, G, 12], F32)
        msum = sb("msum", [P, G], F32)
        dev = sb("dev", [P, G, 4], F32)
        vsum = sb("vsum", [P, G], F32)
        var = sb("var", [P, G], F32)
        std = sb("std", [P, G], F32)
        small = sb("small", [P, 4, G], F32)
        rstd = sb("rstd", [P, G], F32)
        nmr = sb("nmr", [P, G], F32)
        wmax = sb("wmax", [P, 6], F32)
        psum = [ctx.enter_context(nc.psum_tensor(f"bank{j}", [P, 512], F32)) for j in range(2 * NB)]

        raw = xs[:, SLOTS - 1, 0:3 * C * 16]
        raw_v = raw.rearrange("p (t c k) -> p t c k", t=3, k=16)
        used = xs[:, SLOTS - 2, 0:NTAP * C]
        used_v = used.rearrange("p (n c) -> p n c", n=NTAP)
        blocks = xs[:, SLOTS - 2, NTAP * C:3 * NTAP * C].bitcast(F16)
        blocks_v = blocks.rearrange("p (n c) -> p n c", n=NPART)

        loaded = [sem(f"loaded{s}") for s in range(SLOTS)]
        stored = [sem(f"stored{s}") for s in range(SLOTS)]
        w_loaded = sem("w_loaded")
        t_cleared = sem("t_cleared")
        cleared = sem("cleared")
        taps_used = sem("taps_used")
        w_step = sem("w_step")
        w_scaled = sem("w_scaled")
        w_high = sem("w_high")
        w_low = sem("w_low")
        bn_done = sem("bn_done")
        stat_step = sem("stat_step")
        var_ready = sem("var_ready")
        std_ready = sem("std_ready")
        norm_ready = sem("norm_ready")
        t_dve = sem("t_dve")
        t_act = sem("t_act")
        t_ready = sem("t_ready")
        hi_ready = sem("hi_ready")
        lo_ready = sem("lo_ready")
        bank_full = sem("bank_full")
        bank_empty = sem("bank_empty")
        bank_added = sem("bank_added")

        def t_image(b, g):
            return view(tn[b], g * T_PAIR + t_at(1, 1), [(TP, HW), (1, HW)])

        def wait_t_free(engine, k):
            if starts(k):
                engine.wait_ge(t_cleared, 1)
            elif starts(k - 1):
                engine.wait_ge(cleared, 3)
            else:
                engine.wait_ge(lo_ready, k - 1)

        def x_image(s, g):
            return xs[:, s, g * PIX:(g + 1) * PIX].rearrange("p (r q) -> p r q", q=HW)

        def t_piece(b, piece):
            r, c, rows, dr, dc, w = piece
            return view(tn[b], t_at(r, c), [(T_PAIR, G), (dr * TP + dc, rows), (1 + r % 2, w)])

        def h_piece(part, piece):
            r, c, rows, dr, dc, w = piece
            step = 27 * (dr // 2) + (dc if r % 2 == 0 else dc // 2)
            return view(part, h_at(r, c), [(H_PAIR, G), (step, rows), (1, w)])

        def unload_weights(engine, copy, first):
            for j in range(first, PREP_BANKS, 2):
                n = min(4, NPART - 4 * j)
                engine.wait_ge(bank_full, j + 1)
                copy(wts[:, 4 * j:4 * j + n, :].rearrange("p n o -> p (n o)"),
                     psum[j][:, 0:n * P]).then_inc(bank_empty, 1)

        block = ctx.enter_context(nc.Block())

        @block.sync
        def _(sp):
            def load(i, s):
                sp.dma_start(xs[:, s, :].rearrange("p (g q) -> p g q", g=G),
                             x_dram[SLOTS * i + s]).then_inc(loaded[s], 16)

            def store(i, s):
                sp.wait_ge(bank_added, NB * (SLOTS * i + s + 1))
                sp.dma_start(out_dram[SLOTS * i + s],
                             xs[:, s, :].rearrange("p (g q) -> p g q", g=G)).then_inc(stored[s], 16)

            load(0, 0)
            for t, w in enumerate((w_up, w_left, w_right)):
                for h in range(2):
                    sp.dma_start(raw[C * h:C * h + C, t * C * 16:(t + 1) * C * 16],
                                 w.rearrange("o c a b -> o (c a b)")).then_inc(w_loaded, 16)
            for t, b in enumerate((b_up, b_left, b_right)):
                for h in range(2):
                    sp.dma_start(bias[C * h:C * h + C, t:t + 1],
                                 b.rearrange("(o a) -> o a", a=1)).then_inc(w_loaded, 16)
            for s in range(1, SLOTS - 2):
                load(0, s)
            sp.wait_ge(bank_empty, PREP_BANKS)
            load(0, SLOTS - 2)

            def step(i, s, more=True):
                store(i, s)
                if s:
                    if more:
                        sp.wait_ge(stored[s - 1], 16 * (i + 1))
                        load(i + 1, s - 1)
                else:
                    if not starts(i):
                        sp.wait_ge(stored[SLOTS - 1], 16 * i)
                    load(i, SLOTS - 1)

            for s in range(SLOTS):
                step(0, s)
            with sp.Fori(1, ROUNDS - 1) as i:
                for s in range(SLOTS):
                    step(i, s)
            for s in range(SLOTS):
                step(ROUNDS - 1, s, more=False)
            for s in range(SLOTS):
                sp.wait_ge(stored[s], 16 * ROUNDS)

        @block.vector
        def _(dve):
            def bn(ahead, g0, g1):
                if ahead is None:
                    return
                i, s = ahead
                if g0 == 0:
                    dve.wait_ge(loaded[s], 16 * (i + 1))
                for g in range(g0, g1):
                    last = nc.vector.bn_stats(stats[:, s % 2, g, 0:6], xs[:, s, g * PIX:(g + 1) * PIX])
                if g1 == G:
                    last.then_inc(bn_done, 1)

            def moments(k, b, ahead=None):
                done = STAT_OPS * k
                means = stats[:, b, :, 1:11:3]
                m2s = stats[:, b, :, 2:12:3]
                nc.vector.stream_shuffle(stats[:, b, :, 6:12], stats[:, b, :, 0:6],
                                         [p ^ 1 for p in range(32)]).then_inc(stat_step, 1)
                bn(ahead, 0, 1)
                dve.wait_ge(stat_step, done + 1)
                nc.vector.reduce_sum(msum[:], means, axis=AX.X).then_inc(stat_step, 1)
                bn(ahead, 1, 2)
                dve.wait_ge(stat_step, done + 2)
                nc.vector.scalar_tensor_tensor(dev[:], msum[:].unsqueeze(2).to_broadcast([P, G, 4]), -0.25, means,
                                               op0=ALU.mult, op1=ALU.add).then_inc(stat_step, 1)
                bn(ahead, 2, 3)
                dve.wait_ge(stat_step, done + 3)
                nc.vector.tensor_tensor(dev[:], dev[:], dev[:], ALU.mult).then_inc(stat_step, 1)
                bn(ahead, 3, 4)
                dve.wait_ge(stat_step, done + 4)
                nc.vector.scalar_tensor_tensor(dev[:], dev[:], float(PIX // 2), m2s,
                                               op0=ALU.mult, op1=ALU.add).then_inc(stat_step, 1)
                bn(ahead, 4, 5)
                dve.wait_ge(stat_step, done + 5)
                nc.vector.reduce_sum(vsum[:], dev[:], axis=AX.X).then_inc(stat_step, 1)
                bn(ahead, 5, 6)
                dve.wait_ge(stat_step, done + 6)
                nc.vector.tensor_scalar(var[:], vsum[:], 1.0 / GROUP, EPS,
                                        ALU.mult, ALU.add).then_inc(var_ready, 1)
                bn(ahead, 6, 7)

            def norms(k, ahead=None):
                done = STAT_OPS * k + 6
                dve.wait_ge(std_ready, k + 1)
                nc.vector.reciprocal(small[:, 0], std[:]).then_inc(stat_step, 1)
                bn(ahead, 7, 8)
                dve.wait_ge(stat_step, done + 1)
                nc.vector.tensor_tensor(small[:, 1], small[:, 0], small[:, 0], ALU.mult).then_inc(stat_step, 1)
                bn(ahead, 8, 9)
                dve.wait_ge(stat_step, done + 2)
                nc.vector.tensor_tensor(small[:, 2], small[:, 1], var[:], ALU.mult).then_inc(stat_step, 1)
                bn(ahead, 9, 10)
                dve.wait_ge(stat_step, done + 3)
                nc.vector.tensor_scalar(small[:, 3], small[:, 2], -0.5 * X_SCALE, 1.5 * X_SCALE,
                                        ALU.mult, ALU.add).then_inc(stat_step, 1)
                dve.wait_ge(stat_step, done + 4)
                nc.vector.tensor_tensor(rstd[:], small[:, 3], small[:, 0], ALU.mult).then_inc(stat_step, 1)
                dve.wait_ge(stat_step, done + 5)
                nc.vector.scalar_tensor_tensor(nmr[:], msum[:], -0.25, rstd[:],
                                               op0=ALU.mult, op1=ALU.mult).then_inc(norm_ready, 1)

            def normalise(k, s, pairs=GD):
                dve.wait_ge(norm_ready, k + 1)
                wait_t_free(dve, k)
                for g in range(pairs):
                    last = nc.vector.tensor_scalar(t_image(s % 2, g), x_image(s, g), rstd[:, g:g + 1], nmr[:, g:g + 1],
                                                   ALU.mult, ALU.add)
                last.then_inc(t_dve, 1)

            def wrap(k, b, more):
                dve.wait_ge(t_dve, k + 1)
                dve.wait_ge(t_act, k + 1)
                for n, (dst, src, dims) in enumerate(WRAPS):
                    if more and n == len(WRAPS) - 1:
                        dve.wait_ge(bn_done, k + 2)
                    last = nc.vector.tensor_copy(view(tn[b], dst, [(T_PAIR, G)] + [(d, n) for d, _, n in dims]),
                                                 view(tn[b], src, [(T_PAIR, G)] + [(d, n) for _, d, n in dims]))
                last.then_inc(t_ready, 1)

            def step(i, s, more=True):
                k = SLOTS * i + s
                ahead = (i, s + 1) if s < SLOTS - 1 else (i + 1, 0)
                if not more:
                    ahead = None
                moments(k, s % 2, ahead)
                norms(k, ahead)
                normalise(k, s)
                bn(ahead, 10, G)
                wrap(k, s % 2, more)

            nc.vector.memset(tn[0][:], 0.0).then_inc(t_cleared, 1)
            bn((0, 0), 0, G)
            dve.wait_ge(bn_done, 1)
            moments(0, 0)
            dve.wait_ge(taps_used, 1)
            nc.vector.reduce_max(wmax[:, 0:1], used, axis=AX.X, apply_absolute_value=True).then_inc(w_step, 1)
            dve.wait_ge(w_step, 1)
            nc.vector.tensor_scalar(wmax[:, 1:2], wmax[:, 0:1], 1e-30, None, ALU.max).then_inc(w_step, 1)
            dve.wait_ge(w_step, 2)
            nc.vector.tensor_scalar(wmax[:, 2:3].bitcast(I32), wmax[:, 1:2].bitcast(I32), 0x7F800000, None,
                                    ALU.bitwise_and).then_inc(w_step, 1)
            dve.wait_ge(w_step, 3)
            nc.vector.reciprocal(wmax[:, 3:4], wmax[:, 2:3]).then_inc(w_step, 1)
            nc.vector.tensor_scalar(wmax[:, 5:6], wmax[:, 2:3], 1.0 / (W_SCALE * X_SCALE), None,
                                    ALU.mult).then_inc(w_step, 1)
            dve.wait_ge(w_step, 5)
            nc.vector.tensor_scalar(wmax[:, 4:5], wmax[:, 3:4], W_SCALE, None, ALU.mult).then_inc(w_step, 1)
            dve.wait_ge(w_step, 6)
            nc.vector.tensor_scalar(used, used, wmax[:, 4:5], None, ALU.mult).then_inc(w_scaled, 1)
            norms(0)
            normalise(0, 0, GD0)
            wrap(0, 0, False)
            unload_weights(dve, nc.vector.tensor_copy, 0)
            bn((0, 1), 0, G)
            dve.wait_ge(bn_done, 2)

            for s in range(1, SLOTS):
                step(0, s)
            with dve.Fori(1, ROUNDS - 1) as i:
                for s in range(SLOTS):
                    step(i, s)
            for s in range(SLOTS):
                step(ROUNDS - 1, s, more=s < SLOTS - 1)

        @block.scalar
        def _(act):
            def root(k):
                act.wait_ge(var_ready, k + 1)
                nc.scalar.activation(std[:], var[:], ACT.Sqrt).then_inc(std_ready, 1)

            def normalise(k, s, g0):
                act.wait_ge(norm_ready, k + 1)
                wait_t_free(act, k)
                for g in range(g0, G):
                    last = nc.scalar.activation(t_image(s % 2, g), x_image(s, g), ACT.Identity,
                                                bias=nmr[:, g:g + 1], scale=rstd[:, g:g + 1])
                last.then_inc(t_act, 1)

            def high(k, b):
                act.wait_ge(t_ready, k + 1)
                act.wait_ge(bank_full, PREP_BANKS + NB * (k - 1))
                for piece in PIECES:
                    last = nc.scalar.copy(h_piece(hi[b], piece), t_piece(b, piece))
                last.then_inc(hi_ready, 1)

            def evacuate(k, b, j):
                act.wait_ge(bank_full, PREP_BANKS + NB * k + j + 1)
                if not starts(k):
                    act.wait_ge(bank_added, NB * (k - 1) + j + 1)
                at = 0
                for n, rect in enumerate(BANKS[j]):
                    cols = rect[3] * rect[6] * G
                    if n and rect[0] == BANKS[j][n - 1][0]:
                        continue
                    cols = sum(q[3] * q[6] * G for q in BANKS[j][n:] if q[0] == rect[0])
                    last = nc.scalar.activation(res[:, BANK_AT[j] + at:BANK_AT[j] + at + cols],
                                                psum[NB * b + j][:, at:at + cols], ACT.Identity,
                                                bias=bias[:, rect[0]:rect[0] + 1], scale=wmax[:, 5:6])
                    at += cols
                last.then_inc(bank_empty, 1)

            def step(i, s, old=True):
                k = SLOTS * i + s
                root(k)
                if old:
                    evacuate(k - LAG, s % 2, 0)
                    evacuate(k - LAG, s % 2, 1)
                normalise(k, s, GD)
                if old:
                    evacuate(k - LAG, s % 2, 2)
                    evacuate(k - LAG, s % 2, 3)
                high(k, s % 2)

            act.wait_ge(w_loaded, 16 * 12)
            for t in range(3):
                for n, (a, b) in enumerate(TAPS[t]):
                    last = nc.scalar.copy(used_v[:, t * NT + n], raw_v[:, t, :, 4 * a + b])
            last.then_inc(taps_used, 1)
            root(0)
            act.wait_ge(w_scaled, 1)
            act.wait_ge(cleared, 1)
            for h in range(2):
                rows = slice(C * h, C * h + C)
                last = nc.scalar.copy(blocks_v[rows, 0:NTAP, rows], used_v[rows])
            last.then_inc(w_high, 1)
            normalise(0, 0, GD0)
            act.wait_ge(cleared, 2)
            high(0, 0)
            unload_weights(act, nc.scalar.copy, 1)

            for s in range(1, SLOTS):
                step(0, s, old=s >= LAG)
            with act.Fori(1, ROUNDS) as i:
                for s in range(SLOTS):
                    step(i, s)
            for k in range(NCHUNK - LAG, NCHUNK):
                for j in range(NB):
                    evacuate(k, k % 2, j)

        @block.gpsimd
        def _(pool):
            nc.gpsimd.memset(ident[:], 0.0)
            nc.gpsimd.memset(blocks.bitcast(F32), 0.0).then_inc(cleared, 1)
            pool.wait_ge(cleared, 1)
            nc.gpsimd.affine_select(out=ident[:], in_=ident[:], compare_op=ALU.not_equal, fill=1.0,
                                    base=0, pattern=[[-1, P]], channel_multiplier=1)
            nc.gpsimd.memset(hi[0][:].bitcast(F32), 0.0)
            nc.gpsimd.memset(lo[0][:].bitcast(F32), 0.0).then_inc(cleared, 1)
            nc.gpsimd.memset(tn[1][:], 0.0)
            nc.gpsimd.memset(hi[1][:].bitcast(F32), 0.0)
            nc.gpsimd.memset(lo[1][:].bitcast(F32), 0.0).then_inc(cleared, 1)

            pool.wait_ge(cleared, 3)
            pool.wait_ge(w_high, 1)
            for h in range(2):
                rows = slice(C * h, C * h + C)
                nc.gpsimd.tensor_tensor(blocks_v[rows, NTAP:NPART, rows], used_v[rows],
                                        blocks_v[rows, 0:NTAP, rows], ALU.subtract).then_inc(w_low, 1)
                pool.wait_ge(w_low, h + 1)

            def low(k, b):
                pool.wait_ge(hi_ready, k + 1)
                for piece in PIECES:
                    last = nc.gpsimd.tensor_tensor(h_piece(lo[b], piece), t_piece(b, piece),
                                                   h_piece(hi[b], piece), ALU.subtract)
                last.then_inc(lo_ready, 1)

            def add(k, s, j):
                pool.wait_ge(bank_empty, PREP_BANKS + NB * k + j + 1)
                at = BANK_AT[j]
                for t, r0, c0, rows, dr, dc, w, kept in BANKS[j]:
                    x0 = s * G * PIX + HW * (2 * r0 + OUT_AT[t][0]) + 2 * c0 + OUT_AT[t][1]
                    xstep = 2 * HW * dr + 2 * dc
                    pieces = [(0, rows, 0, kept[0])]
                    if kept[-1] > kept[0]:
                        pieces.append((rows - 1, 1, kept[0], kept[-1] - kept[0]))
                    for row, nrow, col, width in pieces:
                        onto = view(xs, x0 + row * xstep + 2 * col, [(PIX, G), (xstep, nrow), (2, width)])
                        last = nc.gpsimd.tensor_tensor(
                            onto, view(res, at + row * w + col, [(rows * w, G), (w, nrow), (1, width)]),
                            onto, ALU.add)
                    at += rows * w * G
                last.then_inc(bank_added, 1)

            def step(i, s, old=True):
                k = SLOTS * i + s
                if old:
                    for j in range(NB):
                        add(k - LAG, (s - LAG) % SLOTS, j)
                low(k, s % 2)

            for s in range(SLOTS):
                step(0, s, old=s >= LAG)
            with pool.Fori(1, ROUNDS) as i:
                for s in range(SLOTS):
                    step(i, s)
            for k in range(NCHUNK - LAG, NCHUNK):
                for j in range(NB):
                    add(k, k % SLOTS, j)

        @block.tensor
        def _(pe):
            pe.wait_ge(w_low, 2)
            pe.wait_ge(cleared, 2)
            for j in range(PREP_BANKS):
                for n in range(4 * j, min(4 * j + 4, NPART)):
                    last = nc.tensor.matmul(psum[j][:, (n - 4 * j) * P:(n - 4 * j + 1) * P], blocks_v[:, n, :],
                                            ident[:], start=True, stop=True)
                last.then_inc(bank_full, 1)
            pe.wait_ge(bank_empty, PREP_BANKS)

            def taps(part, rect, tap):
                t, r0, c0, rows, dr, dc, w, _ = rect
                r, c = 2 * r0 + tap[0], 2 * c0 + tap[1]
                odd = r % 2
                step = 27 * dr + (dc if odd else 2 * dc)
                return view(part, h_at(r, c), [(H_PAIR, G), (step, rows), (1 if odd else 2, w)])

            def convolve(k, b):
                pe.wait_ge(lo_ready, k + 1)
                for j, rects in enumerate(BANKS):
                    pe.wait_ge(bank_empty, NB * k + j + 1)
                    at = 0
                    for q, rect in enumerate(rects):
                        cols = rect[3] * rect[6] * G
                        for n, tap in enumerate(TAPS[rect[0]]):
                            for m, (wpart, xpart) in enumerate(((0, hi[b]), (0, lo[b]), (1, hi[b]))):
                                last = nc.tensor.matmul(
                                    psum[NB * b + j][:, at:at + cols], wts[:, wpart * NTAP + NT * rect[0] + n, :],
                                    taps(xpart, rect, tap), start=(q == 0 and n == 0 and m == 0),
                                    stop=(n == NT - 1 and m == 2), skip_group_check=True)
                        at += cols
                    last.then_inc(bank_full, 1)

            with pe.Fori(0, NCHUNK // 2) as i:
                for b in range(2):
                    convolve(2 * i + b, b)


_INS = ["x", "L0_conv_w_up", "L0_conv_b_up", "L0_conv_w_left", "L0_conv_b_left", "L0_conv_w_right", "L0_conv_b_right"]


def kernel(**inputs):
    import concourse.bacc as _bacc
    from concourse.bass_utils import run_bass_kernel_spmd as _run

    nc = _bacc.Bacc("TRN2", target_bir_lowering=False, num_devices=1,
                     dynamic_dma_scratch_size=4096)
    arrays, args = {}, []
    for name in _INS:
        a = np.ascontiguousarray(inputs[name])
        arrays[f"in_{name}"] = a
        args.append(nc.dram_tensor(f"in_{name}", a.shape, mybir.dt.from_np(a.dtype), kind="ExternalInput").ap())
    shape = arrays["in_x"].shape
    out = nc.dram_tensor("out_0", shape, F32, kind="ExternalOutput").ap()
    hex_conv(nc, *args, out)
    r = _run(nc, [arrays], core_ids=[0])
    return r.results[0]["out_0"]
```

```python
from contextlib import ExitStack

import concourse.bass as bass
import numpy as np
from concourse import mybir

F32 = mybir.dt.float32
F16 = mybir.dt.float16
I32 = mybir.dt.int32
ALU = mybir.AluOpType
ACT = mybir.ActivationFunctionType
AX = mybir.AxisListType

P = 128
B, C, HW = 2048, 64, 16
PIX = HW * HW
G = 16
NCHUNK = B // (2 * G)
SLOTS = 8
ROUNDS = NCHUNK // SLOTS
LAG = 2
GD = 8
GD0 = 9
EPS = 1e-5
GROUP = 2 * PIX

X_SCALE = 2048.0
W_SCALE = 512.0

TP = 18
T_PAIR = 17 * TP
H_PAIR = 8 * 27 + 9


def t_at(r, c):
    return TP * (r - 1) + c


def h_at(r, c):
    return 27 * (r // 2) - 18 + c if r % 2 == 0 else 27 * (r // 2) + (c - 1) // 2


UP, LEFT, RIGHT = range(3)
TAPS = [
    [(0, 0), (0, 1), (1, 1), (2, 1), (2, 2)],
    [(1, 1), (2, 0), (2, 1), (2, 2), (3, 1)],
    [(1, 1), (2, 1), (2, 2), (2, 3), (3, 3)],
]
OUT_AT = [(0, 0), (1, 0), (1, 1)]
NT = 5
NTAP = 3 * NT
NPART = 2 * NTAP

BANKS = [
    [(UP, 2, 0, 3, 2, 1, 6, (6,)), (UP, 3, 0, 2, 2, 1, 6, (6,))],
    [(LEFT, 2, 0, 2, 2, 1, 6, (6,)), (LEFT, 3, 1, 2, 2, 1, 6, (6,)), (LEFT, 1, 1, 2, 5, 2, 4, (4,))],
    [(RIGHT, 2, 0, 1, 2, 1, 6, (6,)), (RIGHT, 4, 1, 1, 2, 1, 7, (7,)), (RIGHT, 3, 0, 2, 2, 1, 6, (6,)), (RIGHT, 0, 1, 2, 7, 3, 2, (2,))],
    [(UP, 1, 1, 2, 6, 3, 3, (3,)), (LEFT, 0, 1, 2, 7, 4, 2, (2,)), (RIGHT, 1, 0, 2, 5, 3, 4, (4,))],
]
NB = len(BANKS)
BANK_COLS = [sum(r[3] * r[6] for r in rects) * G for rects in BANKS]
BANK_AT = [sum(BANK_COLS[:j]) for j in range(NB)]

PIECES = [
    (4, -1, 6, 2, 1, 14), (3, -1, 4, 4, 2, 8), (5, 1, 3, 4, 2, 7),
    (2, 2, 2, 14, 7, 6), (1, 3, 2, 16, 8, 2), (10, 16, 1, 2, 1, 1),
]

DVE_PIECES = 3

ZERO_CELLS = [(6, 14, 2), (10, 17, 1)]
QUARTER = G // 4

WRAPS = [
    (t_at(1, 3), t_at(13, 15), [(13 * TP + 13, -11 * TP - 11, 2), (TP - 1, TP - 1, 4)]),
    (t_at(1, 5), t_at(13, 5), [(13 * TP, -11 * TP, 2), (TP + 2, TP + 2, 4)]),
    (t_at(6, 0), t_at(6, 12), [(13, -11, 2), (2 * TP + 1, 2 * TP + 1, 4)]),
    (t_at(4, 1), t_at(16, 13), [(10 * TP + 5, -14 * TP - 7, 2), (9, -3, 2)]),
    (t_at(7, 13), t_at(7, 1), [(4 * TP + 2, 4 * TP + 2, 2)]),
]

PREP_BANKS = 8
STAT_OPS = 11


def starts(k):
    return isinstance(k, int) and k == 0


def view(tensor, at, dims, first=0, parts=P):
    full = tensor[:, ]
    row = full.ap[0][0]
    return bass.AP(full.tensor, full.offset + first * row + at, [[row, parts]] + [list(d) for d in dims])


def hex_conv(nc, x, w_up, b_up, w_left, b_left, w_right, b_right, out):
    ctx = ExitStack()
    with ctx:
        def sb(name, shape, dt):
            return ctx.enter_context(nc.sbuf_tensor(name, shape, dt))

        def sem(name):
            return ctx.enter_context(nc.semaphore(name))

        x_dram = x.rearrange("(n g h) c r q -> n (h c) g (r q)", g=G, h=2)
        out_dram = out.rearrange("(n g h) c r q -> n (h c) g (r q)", g=G, h=2)

        xs = sb("xs", [P, SLOTS, G * PIX], F32)
        tn = [sb(f"tn{b}", [P, G * T_PAIR], F32) for b in range(2)]
        hi = [sb(f"hi{b}", [P, G * H_PAIR], F16) for b in range(2)]
        lo = [sb(f"lo{b}", [P, G * H_PAIR], F16) for b in range(2)]
        wts = sb("wts", [P, NPART, P], F16)
        res = sb("res", [P, sum(BANK_COLS)], F32)
        ident = sb("ident", [C, C], F16)
        bias = sb("bias", [P, 3], F32)
        stats = sb("stats", [P, 2, G, 12], F32)
        msum = sb("msum", [P, G], F32)
        dev = sb("dev", [P, G, 4], F32)
        vsum = sb("vsum", [P, G], F32)
        var = sb("var", [P, G], F32)
        std = sb("std", [P, G], F32)
        warm = sb("warm", [C, 1], F32)
        small = sb("small", [P, 4, G], F32)
        rstd = sb("rstd", [P, G], F32)
        nmr = sb("nmr", [P, G], F32)
        wmax = sb("wmax", [P, 6], F32)
        psum = [ctx.enter_context(nc.psum_tensor(f"bank{j}", [P, 512], F32)) for j in range(2 * NB)]

        raw = xs[0:C, SLOTS - 1, 0:3 * C * 16]
        raw_v = raw.rearrange("p (t c k) -> p t c k", t=3, k=16)
        used = xs[0:C, SLOTS - 2, 0:NTAP * C]
        used_v = used.rearrange("p (n c) -> p n c", n=NTAP)
        parts = xs[0:C, SLOTS - 2, NTAP * C:(2 * NTAP + 1) * C].bitcast(F16)

        loaded = [sem(f"loaded{s}") for s in range(SLOTS)]
        stored = [sem(f"stored{s}") for s in range(SLOTS)]
        w_loaded = sem("w_loaded")
        b_loaded = sem("b_loaded")
        quarter = [sem(f"quarter{n}") for n in range(3)]
        cleared = sem("cleared")
        taps_used = sem("taps_used")
        w_step = sem("w_step")
        w_high = sem("w_high")
        w_low = sem("w_low")
        bn_done = sem("bn_done")
        stat_step = sem("stat_step")
        var_ready = sem("var_ready")
        std_ready = sem("std_ready")
        norm_ready = sem("norm_ready")
        t_dve = sem("t_dve")
        t_act = sem("t_act")
        t_ready = sem("t_ready")
        hi_ready = sem("hi_ready")
        lo_ready = sem("lo_ready")
        lo_small = sem("lo_small")
        bank_full = sem("bank_full")
        bank_empty = sem("bank_empty")
        bank_added = sem("bank_added")

        def t_image(b, g):
            return view(tn[b], g * T_PAIR + t_at(1, 1), [(TP, HW), (1, HW)])

        def wait_t_free(engine, k):
            if starts(k) or starts(k - 1):
                engine.wait_ge(cleared, 2)
            else:
                engine.wait_ge(lo_ready, k - 1)

        def x_image(s, g):
            return xs[:, s, g * PIX:(g + 1) * PIX].rearrange("p (r q) -> p r q", q=HW)

        def t_piece(b, piece):
            r, c, rows, dr, dc, w = piece
            return view(tn[b], t_at(r, c), [(T_PAIR, G), (dr * TP + dc, rows), (1 + r % 2, w)])

        def h_piece(part, piece):
            r, c, rows, dr, dc, w = piece
            step = 27 * (dr // 2) + (dc if r % 2 == 0 else dc // 2)
            return view(part, h_at(r, c), [(H_PAIR, G), (step, rows), (1, w)])

        block = ctx.enter_context(nc.Block())

        @block.sync
        def _(sp):
            def load(i, s):
                sp.dma_start(xs[:, s, :].rearrange("p (g q) -> p g q", g=G),
                             x_dram[SLOTS * i + s]).then_inc(loaded[s], 16)

            def store(i, s):
                sp.wait_ge(bank_added, NB * (SLOTS * i + s + 1))
                sp.dma_start(out_dram[SLOTS * i + s],
                             xs[:, s, :].rearrange("p (g q) -> p g q", g=G)).then_inc(stored[s], 16)

            for n in range(4):
                pairs = slice(QUARTER * n, QUARTER * (n + 1))
                sp.dma_start(xs[:, 0, :].rearrange("p (g q) -> p g q", g=G)[:, pairs],
                             x_dram[0][:, pairs]).then_inc(quarter[n] if n < 3 else loaded[0], 16)
            for t, w in enumerate((w_up, w_left, w_right)):
                sp.dma_start(raw[:, t * C * 16:(t + 1) * C * 16],
                             w.rearrange("o c a b -> o (c a b)")).then_inc(w_loaded, 16)
            load(0, 1)
            load(0, 2)
            for t, b in enumerate((b_up, b_left, b_right)):
                for h in range(2):
                    sp.dma_start(bias[C * h:C * h + C, t:t + 1],
                                 b.rearrange("(o a) -> o a", a=1)).then_inc(b_loaded, 16)
            sp.wait_ge(w_step, 5)
            sp.dma_start(wmax[C:P, 5:6], wmax[0:C, 5:6]).then_inc(b_loaded, 16)
            for s in range(3, SLOTS - 2):
                load(0, s)
            sp.wait_ge(bank_empty, PREP_BANKS)
            load(0, SLOTS - 2)

            def step(i, s, more=True):
                store(i, s)
                if s:
                    if more:
                        sp.wait_ge(stored[s - 1], 16 * (i + 1))
                        load(i + 1, s - 1)
                else:
                    if not starts(i):
                        sp.wait_ge(stored[SLOTS - 1], 16 * i)
                    load(i, SLOTS - 1)

            for s in range(SLOTS):
                step(0, s)
            with sp.Fori(1, ROUNDS - 1) as i:
                for s in range(SLOTS):
                    step(i, s)
            for s in range(SLOTS - 1):
                step(ROUNDS - 1, s, more=False)
            for half in range(2):
                pairs = slice(G // 2 * half, G // 2 * (half + 1))
                sp.wait_ge(bank_added, NB * (NCHUNK + half))
                sp.dma_start(out_dram[NCHUNK - 1][:, pairs],
                             xs[:, SLOTS - 1, :].rearrange("p (g q) -> p g q", g=G)[:, pairs]
                             ).then_inc(stored[SLOTS - 1], 16)
            for s in range(SLOTS):
                sp.wait_ge(stored[s], 16 * (ROUNDS + (s == SLOTS - 1)))

        @block.vector
        def _(dve):
            def bn(ahead, g0, g1):
                if ahead is None:
                    return
                i, s = ahead
                if g0 == 0:
                    dve.wait_ge(loaded[s], 16 * (i + 1))
                for g in range(g0, g1):
                    last = nc.vector.bn_stats(stats[:, s % 2, g, 0:6], xs[:, s, g * PIX:(g + 1) * PIX])
                if g1 == G:
                    last.then_inc(bn_done, 1)

            def moments(k, b, ahead=None):
                done = STAT_OPS * k
                means = stats[:, b, :, 1:11:3]
                m2s = stats[:, b, :, 2:12:3]
                nc.vector.stream_shuffle(stats[:, b, :, 6:12], stats[:, b, :, 0:6],
                                         [p ^ 1 for p in range(32)]).then_inc(stat_step, 1)
                bn(ahead, 0, 1)
                dve.wait_ge(stat_step, done + 1)
                nc.vector.reduce_sum(msum[:], means, axis=AX.X).then_inc(stat_step, 1)
                bn(ahead, 1, 2)
                dve.wait_ge(stat_step, done + 2)
                nc.vector.scalar_tensor_tensor(dev[:], msum[:].unsqueeze(2).to_broadcast([P, G, 4]), -0.25, means,
                                               op0=ALU.mult, op1=ALU.add).then_inc(stat_step, 1)
                bn(ahead, 2, 3)
                dve.wait_ge(stat_step, done + 3)
                nc.vector.tensor_tensor(dev[:], dev[:], dev[:], ALU.mult).then_inc(stat_step, 1)
                bn(ahead, 3, 4)
                dve.wait_ge(stat_step, done + 4)
                nc.vector.scalar_tensor_tensor(dev[:], dev[:], float(PIX // 2), m2s,
                                               op0=ALU.mult, op1=ALU.add).then_inc(stat_step, 1)
                bn(ahead, 4, 5)
                dve.wait_ge(stat_step, done + 5)
                nc.vector.reduce_sum(vsum[:], dev[:], axis=AX.X).then_inc(stat_step, 1)
                bn(ahead, 5, 6)
                dve.wait_ge(stat_step, done + 6)
                nc.vector.tensor_scalar(var[:], vsum[:], 1.0 / GROUP, EPS,
                                        ALU.mult, ALU.add).then_inc(var_ready, 1)
                bn(ahead, 6, 7)

            def low_small(k, b):
                dve.wait_ge(hi_ready, k + 1)
                for piece in PIECES[-DVE_PIECES:]:
                    last = nc.vector.tensor_tensor(h_piece(lo[b], piece), t_piece(b, piece),
                                                   h_piece(hi[b], piece), ALU.subtract)
                last.then_inc(lo_small, 1)

            def norms(k, ahead=None, low=None):
                done = STAT_OPS * k + 6
                dve.wait_ge(std_ready, k + 1)
                nc.vector.reciprocal(small[:, 0], std[:]).then_inc(stat_step, 1)
                if low is not None:
                    low_small(k - 1, low)
                bn(ahead, 7, 8)
                dve.wait_ge(stat_step, done + 1)
                nc.vector.tensor_tensor(small[:, 1], small[:, 0], small[:, 0], ALU.mult).then_inc(stat_step, 1)
                bn(ahead, 8, 9)
                dve.wait_ge(stat_step, done + 2)
                nc.vector.tensor_tensor(small[:, 2], small[:, 1], var[:], ALU.mult).then_inc(stat_step, 1)
                bn(ahead, 9, 10)
                dve.wait_ge(stat_step, done + 3)
                nc.vector.tensor_scalar(small[:, 3], small[:, 2], -0.5 * X_SCALE, 1.5 * X_SCALE,
                                        ALU.mult, ALU.add).then_inc(stat_step, 1)
                dve.wait_ge(stat_step, done + 4)
                nc.vector.tensor_tensor(rstd[:], small[:, 3], small[:, 0], ALU.mult).then_inc(stat_step, 1)
                dve.wait_ge(stat_step, done + 5)
                nc.vector.scalar_tensor_tensor(nmr[:], msum[:], -0.25, rstd[:],
                                               op0=ALU.mult, op1=ALU.mult).then_inc(norm_ready, 1)

            def t_pairs(b, s, g0, g1):
                for g in range(g0, g1):
                    last = nc.vector.tensor_scalar(t_image(b, g), x_image(s, g), rstd[:, g:g + 1], nmr[:, g:g + 1],
                                                   ALU.mult, ALU.add)
                return last

            def normalise(k, s, pairs=GD):
                dve.wait_ge(norm_ready, k + 1)
                wait_t_free(dve, k)
                t_pairs(s % 2, s, 0, pairs).then_inc(t_dve, 1)

            def wrap(k, b, more):
                dve.wait_ge(t_dve, k + 1)
                dve.wait_ge(t_act, k + 1)
                for n, (dst, src, dims) in enumerate(WRAPS):
                    if more and n == len(WRAPS) - 1:
                        dve.wait_ge(bn_done, k + 2)
                    last = nc.vector.tensor_copy(view(tn[b], dst, [(T_PAIR, G)] + [(d, n) for d, _, n in dims]),
                                                 view(tn[b], src, [(T_PAIR, G)] + [(d, n) for _, d, n in dims]))
                last.then_inc(t_ready, 1)


            def step(i, s, more=True):
                k = SLOTS * i + s
                ahead = (i, s + 1) if s < SLOTS - 1 else (i + 1, 0)
                if not more:
                    ahead = None
                moments(k, s % 2, ahead)
                norms(k, ahead, None if starts(k - 1) else (s - 1) % 2)
                normalise(k, s)
                bn(ahead, 10, G)
                wrap(k, s % 2, more)

            for n in range(3):
                dve.wait_ge(quarter[n], 16)
                for g in range(QUARTER * n, QUARTER * (n + 1)):
                    nc.vector.bn_stats(stats[:, 0, g, 0:6], xs[:, 0, g * PIX:(g + 1) * PIX])
            dve.wait_ge(loaded[0], 16)
            bn((0, 0), 3 * QUARTER, G)
            dve.wait_ge(bn_done, 1)
            moments(0, 0)
            norms(0)
            dve.wait_ge(norm_ready, 1)
            wait_t_free(dve, 0)
            t_pairs(0, 0, 0, 6)
            dve.wait_ge(taps_used, 1)
            nc.vector.reduce_max(wmax[0:C, 0:1], used, axis=AX.X, apply_absolute_value=True).then_inc(w_step, 1)
            t_pairs(0, 0, 6, 7)
            dve.wait_ge(w_step, 1)
            nc.vector.tensor_scalar(wmax[0:C, 1:2], wmax[0:C, 0:1], 1e-30, None, ALU.max).then_inc(w_step, 1)
            t_pairs(0, 0, 7, 8)
            dve.wait_ge(w_step, 2)
            nc.vector.tensor_scalar(wmax[0:C, 2:3].bitcast(I32), wmax[0:C, 1:2].bitcast(I32), 0x7F800000, None,
                                    ALU.bitwise_and).then_inc(w_step, 1)
            t_pairs(0, 0, 8, GD0).then_inc(t_dve, 1)
            dve.wait_ge(w_step, 3)
            nc.vector.reciprocal(wmax[0:C, 3:4], wmax[0:C, 2:3]).then_inc(w_step, 1)
            nc.vector.tensor_scalar(wmax[0:C, 5:6], wmax[0:C, 2:3], 1.0 / (W_SCALE * X_SCALE), None,
                                    ALU.mult).then_inc(w_step, 1)
            dve.wait_ge(w_step, 5)
            nc.vector.tensor_scalar(wmax[0:C, 4:5], wmax[0:C, 3:4], W_SCALE, None, ALU.mult).then_inc(w_step, 1)
            wrap(0, 0, False)
            bn((0, 1), 0, 2)
            dve.wait_ge(w_step, 6)
            dve.wait_ge(w_high, 1)
            nc.vector.scalar_tensor_tensor(parts[:, (NTAP + 1) * C:(NPART + 1) * C], used, wmax[0:C, 4:5],
                                           parts[:, C:(NTAP + 1) * C],
                                           op0=ALU.mult, op1=ALU.subtract).then_inc(w_low, 1)
            bn((0, 1), 2, G // 2)
            low_small(0, 0)
            bn((0, 1), G // 2, G)
            dve.wait_ge(bn_done, 2)

            for s in range(1, SLOTS):
                step(0, s)
            with dve.Fori(1, ROUNDS - 1) as i:
                for s in range(SLOTS):
                    step(i, s)
            for s in range(SLOTS):
                step(ROUNDS - 1, s, more=s < SLOTS - 1)
            low_small(NCHUNK - 1, (NCHUNK - 1) % 2)

        @block.scalar
        def _(act):
            def root(k):
                act.wait_ge(var_ready, k + 1)
                nc.scalar.activation(std[:], var[:], ACT.Sqrt).then_inc(std_ready, 1)

            def normalise(k, s, g0):
                act.wait_ge(norm_ready, k + 1)
                wait_t_free(act, k)
                for g in range(g0, G):
                    last = nc.scalar.activation(t_image(s % 2, g), x_image(s, g), ACT.Identity,
                                                bias=nmr[:, g:g + 1], scale=rstd[:, g:g + 1])
                last.then_inc(t_act, 1)

            def high(k, b):
                act.wait_ge(t_ready, k + 1)
                if not (starts(k) or starts(k - 1)):
                    act.wait_ge(bank_full, PREP_BANKS + NB * (k - 1))
                for piece in PIECES:
                    last = nc.scalar.copy(h_piece(hi[b], piece), t_piece(b, piece))
                last.then_inc(hi_ready, 1)

            def unload_weights(j):
                act.wait_ge(bank_full, j + 1)
                for h in range(2):
                    rows = slice(C * h, C * h + C)
                    m0, m1 = (1 if h + j == 0 else 0), min(4, NPART + 1 - h - 4 * j)
                    n0 = 4 * j - 1 + h
                    last = nc.scalar.copy(wts[rows, n0 + m0:n0 + m1, rows],
                                psum[j][rows, 0:4 * C].rearrange("p (n o) -> p n o", n=4)[:, m0:m1])
                last.then_inc(bank_empty, 1)

            def evacuate(k, b, j, pairs=G):
                act.wait_ge(bank_full, PREP_BANKS + NB * k + j + 1)
                if not starts(k):
                    act.wait_ge(bank_added, NB * (k - 1) + j + 1)
                at = 0
                for n, rect in enumerate(BANKS[j]):
                    if n and rect[0] == BANKS[j][n - 1][0]:
                        continue
                    cols = sum(q[3] * q[6] * pairs for q in BANKS[j][n:] if q[0] == rect[0])
                    last = nc.scalar.activation(res[:, BANK_AT[j] + at:BANK_AT[j] + at + cols],
                                                psum[NB * b + j][:, at:at + cols], ACT.Identity,
                                                bias=bias[:, rect[0]:rect[0] + 1], scale=wmax[:, 5:6])
                    at += cols
                last.then_inc(bank_empty, 1)

            def step(i, s, old=True):
                k = SLOTS * i + s
                root(k)
                if old:
                    evacuate(k - LAG, s % 2, 0)
                    evacuate(k - LAG, s % 2, 1)
                normalise(k, s, GD)
                if old:
                    evacuate(k - LAG, s % 2, 2)
                    evacuate(k - LAG, s % 2, 3)
                high(k, s % 2)

            act.wait_ge(cleared, 2)
            nc.scalar.activation(warm[:], ident[:, 0:1], ACT.Sqrt)
            root(0)
            act.wait_ge(w_loaded, 16 * 3)
            for t in range(3):
                for n, (a, b) in enumerate(TAPS[t]):
                    last = nc.scalar.copy(used_v[:, t * NT + n], raw_v[:, t, :, 4 * a + b])
            last.then_inc(taps_used, 1)
            normalise(0, 0, GD0)
            act.wait_ge(w_step, 6)
            nc.scalar.activation(parts[:, C:(NTAP + 1) * C], used, ACT.Identity,
                                 scale=wmax[0:C, 4:5]).then_inc(w_high, 1)
            high(0, 0)
            for j in range(PREP_BANKS):
                unload_weights(j)

            step(0, 1, old=False)
            act.wait_ge(b_loaded, 16 * 7)
            for s in range(LAG, SLOTS):
                step(0, s)
            with act.Fori(1, ROUNDS) as i:
                for s in range(SLOTS):
                    step(i, s)
            for k in range(NCHUNK - LAG, NCHUNK + 1):
                for j in range(NB):
                    evacuate(k, k % 2, j, G if k < NCHUNK - 1 else G // 2)

        @block.gpsimd
        def _(pool):
            nc.gpsimd.memset(ident[:], 0.0)
            nc.gpsimd.memset(wts[:].rearrange("p n o -> p (n o)").bitcast(F32), 0.0).then_inc(cleared, 1)
            for at in (0, (NPART + 1) * C):
                nc.gpsimd.memset(parts[:, at:at + C], 0.0)
            for t in tn:
                nc.gpsimd.memset(view(t, t_at(1, 17), [(T_PAIR, G), (TP, HW), (1, 2)]), 0.0)
                nc.gpsimd.memset(view(t, t_at(1, 0), [(T_PAIR, G), (1, 1)]), 0.0)
                nc.gpsimd.memset(view(t, t_at(17, 1), [(T_PAIR, G), (1, TP - 1)]), 0.0)
            for part in (*hi, *lo):
                for r, c, n in ZERO_CELLS:
                    nc.gpsimd.memset(view(part, h_at(r, c), [(H_PAIR, G), (1, n)]), 0.0)
            pool.wait_ge(cleared, 1)
            nc.gpsimd.affine_select(out=ident[:], in_=ident[:], compare_op=ALU.not_equal, fill=1.0,
                                    base=0, pattern=[[-1, C]], channel_multiplier=1).then_inc(cleared, 1)

            def low(k, b):
                pool.wait_ge(hi_ready, k + 1)
                for piece in PIECES[:-DVE_PIECES]:
                    last = nc.gpsimd.tensor_tensor(h_piece(lo[b], piece), t_piece(b, piece),
                                                   h_piece(hi[b], piece), ALU.subtract)
                last.then_inc(lo_ready, 1)

            def add(k, s, j, g0=0, pairs=G):
                pool.wait_ge(bank_empty, PREP_BANKS + NB * k + j + 1)
                at = BANK_AT[j]
                for t, r0, c0, rows, dr, dc, w, kept in BANKS[j]:
                    x0 = (s * G + g0) * PIX + HW * (2 * r0 + OUT_AT[t][0]) + 2 * c0 + OUT_AT[t][1]
                    xstep = 2 * HW * dr + 2 * dc
                    pieces = [(0, rows, 0, kept[0])]
                    if kept[-1] > kept[0]:
                        pieces.append((rows - 1, 1, kept[0], kept[-1] - kept[0]))
                    for row, nrow, col, width in pieces:
                        onto = view(xs, x0 + row * xstep + 2 * col, [(PIX, pairs), (xstep, nrow), (2, width)])
                        last = nc.gpsimd.tensor_tensor(
                            onto, view(res, at + row * w + col, [(rows * w, pairs), (w, nrow), (1, width)]),
                            onto, ALU.add)
                    at += rows * w * pairs
                last.then_inc(bank_added, 1)

            def step(i, s, old=True):
                k = SLOTS * i + s
                if old:
                    for j in range(NB):
                        add(k - LAG, (s - LAG) % SLOTS, j)
                low(k, s % 2)

            for s in range(SLOTS):
                step(0, s, old=s >= LAG)
            with pool.Fori(1, ROUNDS) as i:
                for s in range(SLOTS):
                    step(i, s)
            for j in range(NB):
                add(NCHUNK - 2, SLOTS - 2, j)
            for half in range(2):
                for j in range(NB):
                    add(NCHUNK - 1 + half, SLOTS - 1, j, G // 2 * half, G // 2)

        @block.tensor
        def _(pe):
            pe.wait_ge(w_low, 1)
            pe.wait_ge(cleared, 2)
            for j in range(PREP_BANKS):
                for n in range(4 * j, min(4 * j + 4, NPART + 1)):
                    last = nc.tensor.matmul(psum[j][:, (n - 4 * j) * C:(n - 4 * j + 1) * C],
                                            parts[:, n * C:n * C + P],
                                            ident[:], start=True, stop=True)
                last.then_inc(bank_full, 1)
            pe.wait_ge(bank_empty, PREP_BANKS)

            def taps(part, rect, tap, g0, pairs):
                t, r0, c0, rows, dr, dc, w, _ = rect
                r, c = 2 * r0 + tap[0], 2 * c0 + tap[1]
                odd = r % 2
                step = 27 * dr + (dc if odd else 2 * dc)
                return view(part, g0 * H_PAIR + h_at(r, c), [(H_PAIR, pairs), (step, rows), (1 if odd else 2, w)])

            def convolve(k, b, bank=None, g0=0, pairs=G):
                bank = NB * (b if bank is None else bank)
                for j, rects in enumerate(BANKS):
                    pe.wait_ge(bank_empty, NB * k + j + 1)
                    at = 0
                    for q, rect in enumerate(rects):
                        cols = rect[3] * rect[6] * pairs
                        for n, tap in enumerate(TAPS[rect[0]]):
                            for m, (wpart, xpart) in enumerate(((0, hi[b]), (0, lo[b]), (1, hi[b]))):
                                last = nc.tensor.matmul(
                                    psum[bank + j][:, at:at + cols], wts[:, wpart * NTAP + NT * rect[0] + n, :],
                                    taps(xpart, rect, tap, g0, pairs), start=(q == 0 and n == 0 and m == 0),
                                    stop=(n == NT - 1 and m == 2), skip_group_check=True)
                        at += cols
                    last.then_inc(bank_full, 1)

            def parts_ready(k):
                pe.wait_ge(lo_ready, k + 1)
                pe.wait_ge(lo_small, k + 1)

            with pe.Fori(0, NCHUNK // 2 - 1) as i:
                for b in range(2):
                    parts_ready(2 * i + b)
                    convolve(2 * i + b, b)
            parts_ready(NCHUNK - 2)
            convolve(NCHUNK - 2, 0)
            parts_ready(NCHUNK - 1)
            for half in range(2):
                convolve(NCHUNK - 1 + half, 1, 1 - half, G // 2 * half, G // 2)


_INS = ["x", "L0_conv_w_up", "L0_conv_b_up", "L0_conv_w_left", "L0_conv_b_left", "L0_conv_w_right", "L0_conv_b_right"]


def kernel(**inputs):
    import concourse.bacc as _bacc
    from concourse.bass_utils import run_bass_kernel_spmd as _run

    nc = _bacc.Bacc("TRN2", target_bir_lowering=False, num_devices=1,
                     dynamic_dma_scratch_size=4096)
    arrays, args = {}, []
    for name in _INS:
        a = np.ascontiguousarray(inputs[name])
        arrays[f"in_{name}"] = a
        args.append(nc.dram_tensor(f"in_{name}", a.shape, mybir.dt.from_np(a.dtype), kind="ExternalInput").ap())
    shape = arrays["in_x"].shape
    out = nc.dram_tensor("out_0", shape, F32, kind="ExternalOutput").ap()
    hex_conv(nc, *args, out)
    r = _run(nc, [arrays], core_ids=[0])
    return r.results[0]["out_0"]
```
